# Optimizing a Trainium2 kernel written in Bass

```python
import numpy as np
import jax
import jax.numpy as jnp

def _softmax(x, axis=-1):
    return jax.nn.softmax(x, axis=axis)

def _gelu(x):
    return jax.nn.gelu(x, approximate=True)

def _silu(x):
    return jax.nn.silu(x)

def _sigmoid(x):
    return jax.nn.sigmoid(x)

def _layernorm(x, axis=-1, eps=1e-05):
    m = jnp.mean(x, axis=axis, keepdims=True)
    v = jnp.var(x, axis=axis, keepdims=True)
    return (x - m) / jnp.sqrt(v + eps)

def _scatter_add(tgt, idx, src, axis=0):
    return tgt.at[idx].add(src)

def _segment_sum(src, seg, n):
    return jax.ops.segment_sum(src, seg, n)
kernel_name = 'mk_seq_preln_d1_jaxref_r8_a25577'

def setup_inputs(seed: int=0):
    np.random.seed(seed)
    _w = jnp.asarray

    def _L0_attn_setup():
        import jax, jax.numpy as jnp
        import numpy as np
        import math
        D_MODEL = 256
        N_HEADS = 16
        D_HEAD = 128
        BATCH = 2
        SEQ = 256
        key = jax.random.key(seed)
        ks = jax.random.split(key, 5)
        std = 0.02
        x = jax.random.normal(ks[0], (BATCH, SEQ, D_MODEL), dtype=jnp.float32)
        W_Q = std * jax.random.normal(ks[1], (N_HEADS, D_HEAD, D_MODEL), dtype=jnp.float32)
        W_K = std * jax.random.normal(ks[2], (N_HEADS, D_HEAD, D_MODEL), dtype=jnp.float32)
        W_V = std * jax.random.normal(ks[3], (N_HEADS, D_HEAD, D_MODEL), dtype=jnp.float32)
        W_O = std * jax.random.normal(ks[4], (N_HEADS, D_MODEL, D_HEAD), dtype=jnp.float32)
        return {'x': x, 'W_Q': W_Q, 'W_K': W_K, 'W_V': W_V, 'W_O': W_O}
    _L0_attn_in = _L0_attn_setup()

    def _L0_ffn_setup():
        import jax, jax.numpy as jnp
        import numpy as np
        LN_EPS = 1e-05
        Q_EPS = 1e-05

        def ternary_quantize(w):
            scale = jnp.mean(jnp.abs(w))
            return jnp.clip(jnp.round(w / (scale + Q_EPS)), -1.0, 1.0)

        def layernorm(x, gamma, beta):
            mu = jnp.mean(x, axis=-1, keepdims=True)
            var = jnp.mean(jnp.square(x - mu), axis=-1, keepdims=True)
            return (x - mu) * jax.lax.rsqrt(var + LN_EPS) * gamma + beta
        key = jax.random.key(seed)
        k_x, k_w = jax.random.split(key)
        B, S, D_IN, D_OUT = (4, 256, 256, 256)
        x = jax.random.normal(k_x, (B, S, D_IN), dtype=jnp.float32)
        std = np.sqrt(2.0 / D_OUT).astype(np.float32)
        weight = jax.random.normal(k_w, (D_OUT, D_IN), dtype=jnp.float32) * std
        bias = jnp.zeros((D_OUT,), dtype=jnp.float32)
        ln_gamma = jnp.ones((D_IN,), dtype=jnp.float32)
        ln_beta = jnp.zeros((D_IN,), dtype=jnp.float32)
        return {'x': x, 'weight': weight, 'bias': bias, 'ln_gamma': ln_gamma, 'ln_beta': ln_beta}
    _L0_ffn_in = _L0_ffn_setup()
    _d = {'L0_attn_x': _L0_attn_in['x'], 'L0_attn_W_Q': _L0_attn_in['W_Q'], 'L0_attn_W_K': _L0_attn_in['W_K'], 'L0_attn_W_V': _L0_attn_in['W_V'], 'L0_attn_W_O': _L0_attn_in['W_O'], 'L0_ffn_weight': _L0_ffn_in['weight'], 'L0_ffn_bias': _L0_ffn_in['bias'], 'L0_ffn_ln_gamma': _L0_ffn_in['ln_gamma'], 'L0_ffn_ln_beta': _L0_ffn_in['ln_beta']}
    _x0 = _d['L0_attn_x']
    _d['L0_attn_x'] = jax.random.normal(jax.random.fold_in(jax.random.key(seed), 1), (2, 1024, 256), dtype=_x0.dtype)
    del _x0
    return _d

def reference(L0_attn_x, L0_attn_W_Q, L0_attn_W_K, L0_attn_W_V, L0_attn_W_O, L0_ffn_weight, L0_ffn_bias, L0_ffn_ln_gamma, L0_ffn_ln_beta):

    def _L0_attn_ref(x, W_Q, W_K, W_V, W_O):
        import jax, jax.numpy as jnp
        import numpy as np
        import math
        D_MODEL = 256
        N_HEADS = 16
        D_HEAD = 128
        BATCH = 2
        SEQ = 256
        d_head = W_Q.shape[1]
        seq_len = x.shape[1]
        scale = 1.0 / math.sqrt(d_head)
        q = jnp.einsum('bsd,hed->bhse', x, W_Q)
        k = jnp.einsum('bsd,hed->bhse', x, W_K)
        v = jnp.einsum('bsd,hed->bhse', x, W_V)
        scores = jnp.einsum('bhse,bhme->bhsm', q, k) * scale
        causal = jnp.triu(jnp.ones((seq_len, seq_len), dtype=bool), k=1)
        scores = jnp.where(causal, jnp.float32(-1000000000.0), scores)
        pattern = jax.nn.softmax(scores, axis=-1)
        z = jnp.einsum('bhsm,bhme->bhse', pattern, v)
        out = jnp.einsum('bhse,hde->bsd', z, W_O)
        return out

    def _L0_ffn_ref(x, weight, bias, ln_gamma, ln_beta):
        import jax, jax.numpy as jnp
        import numpy as np
        LN_EPS = 1e-05
        Q_EPS = 1e-05

        def ternary_quantize(w):
            scale = jnp.mean(jnp.abs(w))
            return jnp.clip(jnp.round(w / (scale + Q_EPS)), -1.0, 1.0)

        def layernorm(x, gamma, beta):
            mu = jnp.mean(x, axis=-1, keepdims=True)
            var = jnp.mean(jnp.square(x - mu), axis=-1, keepdims=True)
            return (x - mu) * jax.lax.rsqrt(var + LN_EPS) * gamma + beta
        xn = layernorm(x, ln_gamma, ln_beta)
        w_q = ternary_quantize(weight)
        return jnp.einsum('bsi,oi->bso', xn, w_q) + bias
    x = L0_attn_x
    x = x + _L0_attn_ref(_layernorm(x, axis=-1), L0_attn_W_Q, L0_attn_W_K, L0_attn_W_V, L0_attn_W_O)
    x = x + _L0_ffn_ref(_layernorm(x, axis=-1), L0_ffn_weight, L0_ffn_bias, L0_ffn_ln_gamma, L0_ffn_ln_beta)
    return x

_drawn_inputs = setup_inputs


def setup_inputs(seed=0):
    import zlib

    import numpy as np

    out = dict(_drawn_inputs(seed))
    spreads = {'L0_ffn_bias': (0.0, 0.8), 'L0_ffn_ln_gamma': (1.0, 0.2), 'L0_ffn_ln_beta': (0.0, 0.1)}
    factors = {'L0_attn_W_Q': 8.0, 'L0_attn_W_K': 8.0}
    for name, (base, spread) in spreads.items():
        noise = np.random.default_rng([zlib.crc32(name.encode()), seed]).standard_normal(out[name].shape)
        drawn = base * np.exp(spread * noise) if base else spread * noise
        out[name] = jnp.asarray(drawn.astype(out[name].dtype))
    for name, factor in factors.items():
        out[name] = (out[name] * factor).astype(out[name].dtype)
    return out
```

```python
from contextlib import ExitStack

import concourse.bass as bass
from concourse import mybir

F32 = mybir.dt.float32
F32R = mybir.dt.float32r
BF16 = mybir.dt.bfloat16
ALU = mybir.AluOpType
ACT = mybir.ActivationFunctionType
AX_X = mybir.AxisListType.X
AX_XY = mybir.AxisListType.XY

P = 128
BANK = 512
LN_EPS = 1e-5
Q_EPS = 1e-5
MASKED = -1e30

HI, LO = 0, 1
PASSES = ((HI, LO), (LO, HI), (HI, HI))

NO_JOB = ("stats", "rstd", "norm", "wabs", "next", "pv_part")
NEXT = ("next", 0)
NO_SPLIT = ("o", "o_own", "wsum", "bw", "ff")
PROLOGUE = (
    ("stats", 0), ("stats", 1), ("rstd", (0, 1)), ("norm", 0), ("rstd", (1, 1)), ("x", (0, 0)), ("x", (0, 1)),
    ("norm", 1), ("qk", 0), ("qk", 2), ("x", (1, 0)), ("x", (1, 1)), ("qk", 1), ("qk", 3),
    ("v", 0), ("stats", 2), ("v", 1), ("stats", 3), ("v", 2), ("rstd", (2, 2)), ("v", 3),
)
UNIT = (
    (NEXT, ("qk", 0)),
    (("pv_part", 1), NEXT),
    (("pv", 1), NEXT, ("o", 0)),
    (("qk", 2), NEXT, ("o", 1)),
    (("qk", 1), NEXT),
    (NEXT, ("o", 2)),
    (("qk", 3), ("v", 0), NEXT, ("o", 3), ("v", 1)),
    (NEXT, ("pv", 0)),
)
FIRST_UNIT = (
    (NEXT, ("norm", 2), ("x", (2, 0)), ("x", (2, 1))),
    (NEXT, ("norm", 3), ("x", (3, 0)), ("x", (3, 1))),
    (NEXT, ("qk", 0),),
    (NEXT, ("qk", 1),),
    (NEXT, ("qk", 2),),
    (NEXT, ("pv", 0),),
    (NEXT, ("qk", 3),),
    (NEXT, ("v", 0), ("v", 1)),
)
LAST_BUT_ONE = (
    (NEXT, ("pv_part", 1), ("pv", 1)),
    (NEXT, ("o", 0), ("o", 1), ("wabs", 0)),
    (NEXT, ("qk", 0),),
    (NEXT, ("o", 2), ("o", 3), ("qk", 1)),
    (NEXT, ("qk", 2), ("wsum", 0), ("stats", 0)),
    (NEXT, ("pv", 0), ("stats", 1), ("rstd", (0, 2))),
    (NEXT, ("qk", 3), ("bw", 0), ("norm", 0)),
    (NEXT, ("xf", (0, 0)), ("xf", (0, 1)), ("norm", 1)),
)
LAST_UNIT = (
    (NEXT, ("pv_part", 1), ("pv", 1)),
    (NEXT, ("o", 0), ("o", 1), ("xf", (1, 0))),
    (NEXT, ("xf", (1, 1)), ("ff", (0, 0))),
    (NEXT, ("o", 2), ("o", 3), ("ff", (0, 1))),
    (NEXT, ("ff", (1, 0)),),
    (NEXT, ("pv", 0),),
    (NEXT, ("ff", (1, 1)),),
    (NEXT, ("o_own", 0), ("o_own", 1)),
)
EPILOGUE = (
    ("stats", 2), ("pv_part", 1), ("pv", 1), ("rstd", (2, 1)), ("norm", 2), ("o", 2), ("o", 3), ("xf", (2, 0)), ("xf", (2, 1)),
    ("stats", 3), ("rstd", (3, 1)), ("norm", 3), ("ff", (2, 0)), ("ff", (2, 1)),
    ("xf", (3, 0)), ("xf", (3, 1)), ("ff", (3, 0)), ("ff", (3, 1)),
)


def jobs_in(items):
    return sum(kind not in NO_JOB for kind, _ in items)


def splits_in(items):
    return sum(kind not in NO_JOB + NO_SPLIT for kind, _ in items)


def flat(unit):
    return [item for slot in unit for item in slot]


def attention_ffn(nc, x, wq, wk, wv, wo, wf, gamma, beta, bias, out):
    TOK, D = x.shape
    PAIRS = wq.shape[0]
    B = 2
    S = TOK // B
    E = P
    KD = D // P
    NT = TOK // P
    QT = S // P
    HALF = QT // 2
    UNITS = 2 * B
    LAST = PAIRS - 1
    SCALE = float(E) ** -0.5
    assert (D, E, QT, KD, S) == (256, P, 8, 2, 2 * BANK)

    x_v = x.rearrange("(n p) d -> p n d", p=P)
    out_v = out.rearrange("(n p) d -> p n d", p=P)

    def banks(t):
        return -(-(t + 1) // 4)

    GROUPS = sum(banks(t) for t in range(QT))

    def is_first(it):
        return isinstance(it, int) and it == 0

    def plan(it, k):
        if is_first(it) and k == 0:
            return FIRST_UNIT
        if isinstance(it, int) and it == LAST and k >= UNITS - 2:
            return (LAST_BUT_ONE, LAST_UNIT)[k - (UNITS - 2)]
        return UNIT

    def has_previous(it, k):
        return k > 0 or not is_first(it)

    def before(it, count):
        if is_first(it):
            return count(PROLOGUE)
        return it * (UNITS * count(flat(UNIT))) + (count(PROLOGUE) + count(flat(FIRST_UNIT)) - count(flat(UNIT)))

    def odd(it):
        return jobs_in(PROLOGUE) % 2 if is_first(it) else before(1, jobs_in) % 2

    assert UNITS * jobs_in(flat(UNIT)) % 2 == 0 and GROUPS % 2 == 0

    def job_at(it, k, item):
        n = 0
        for u in range(k + 1):
            for i in flat(plan(it, u)):
                n += i[0] not in NO_JOB
                if u == k and i == item:
                    return n
        raise AssertionError(item)

    with ExitStack() as ctx:
        def sb(name, shape, dt):
            return ctx.enter_context(nc.sbuf_tensor(name, shape, dt))

        def pb(name, shape, dt):
            return ctx.enter_context(nc.psum_tensor(name, shape, dt))

        def sem(name):
            return ctx.enter_context(nc.semaphore(name))

        scores = pb("scores", [P, 2, 2 * BANK], F32)
        turned = pb("turned", [P, 2, BANK], F32)
        ring = pb("ring", [P, 2, BANK], F32)

        xT = sb("xT", [P, 2, KD, TOK], F32R)
        qT = sb("qT", [P, 2, 2, S], F32R)
        kT = sb("kT", [P, 2, 2, S], F32R)
        v = sb("v", [P, B, 2, QT, 2 * E], F32R)
        pT0 = sb("pT0", [P, 2, HALF, BANK], F32R)
        pT1 = sb("pT1", [P, 2, QT, BANK], F32R)
        zT = sb("zT", [P, 2, S], F32R)
        acc = sb("acc", [P, NT, D], F32)
        probs = sb("probs", [P, 2, S], F32)
        norm = sb("norm", [P, 4, D], F32)
        wq_s = sb("wq_s", [P, 2, KD, 2 * E], F32R)
        wk_s = sb("wk_s", [P, 2, KD, 2 * E], F32R)
        wv_s = sb("wv_s", [P, 2, KD, 2 * E], F32R)
        wo_s = sb("wo_s", [P, 2, 2, D], F32R)
        wq_raw = sb("wq_raw", [P, KD, 2 * E], F32)
        wk_raw = sb("wk_raw", [P, KD, 2 * E], F32)
        wv_raw = sb("wv_raw", [P, KD, 2 * E], F32)
        wo_raw = wv_raw
        wf_s = sb("wf_s", [P, KD, D], F32R)
        bias_s = sb("bias_s", [P, D], F32)
        gamma_s = sb("gamma_s", [P, KD], F32)
        beta_s = sb("beta_s", [P, KD], F32)
        ident = sb("ident", [P, P], F32)
        ident_b = sb("ident_b", [P, P], BF16)
        mask = sb("mask", [P, P], BF16)
        one = sb("one", [P, 1], F32)
        zero = sb("zero", [P, 1], F32)
        eps = sb("eps", [P, 2], F32)
        negmax = sb("negmax", [P, 2], F32)
        rowsum = sb("rowsum", [P, 2, QT], F32)
        inv = sb("inv", [P, 2, QT], F32)
        stats = sb("stats", [P, NT, 6], F32)
        mv = sb("mv", [P, NT, 2], F32)
        std = sb("std", [P, NT], F32)
        rstd = sb("rstd", [P, NT], F32)
        wabs = sb("wabs", [P, 1], F32)
        thr = sb("thr", [P, 2], F32)

        wf_raw = wq_raw[:, :, 0:D]
        wf_neg = wk_raw[:, :, 0:D]

        x_in = [sem(f"x_in{g}") for g in range(4)]
        small_in = sem("small_in")
        wq_in, wk_in, wv_in, wo_in, wf_in = sem("wq_in"), sem("wk_in"), sem("wv_in"), sem("wo_in"), sem("wf_in")
        wq_ready, wk_ready, wv_ready, wo_ready = sem("wq_ready"), sem("wk_ready"), sem("wv_ready"), sem("wo_ready")
        hi_done = sem("hi_done")
        const_ready = sem("const_ready")
        dve_const = sem("dve_const")
        scores_ready = sem("scores_ready")
        max_ready = sem("max_ready")
        probs_ready = sem("probs_ready")
        turned_ready = sem("turned_ready")
        phi_ready = sem("phi_ready")
        plo_ready = sem("plo_ready")
        job_done = sem("job_done")
        jhi_ready = sem("jhi_ready")
        job_taken = sem("job_taken")
        inv_ready = sem("inv_ready")
        ln_step = sem("ln_step")
        std_ready = sem("std_ready")
        norm_ready = sem("norm_ready")
        wabs_ready = sem("wabs_ready")
        tern_step = sem("tern_step")
        wf_ready = sem("wf_ready")
        resid_ready = sem("resid_ready")
        stored = sem("stored")

        def f32(ap):
            return ap.bitcast(F32)

        ffn_job = {}
        n = before(LAST, jobs_in)
        for item in [i for k in range(UNITS) for i in flat(plan(LAST, k))] + list(EPILOGUE):
            n += item[0] not in NO_JOB
            if item[0] == "ff":
                ffn_job[item[1]] = n

        block = ctx.enter_context(nc.Block())

        @block.sync
        def _(sp):
            weights = ((wv_raw, wv, wv_in, wo_ready, 0), (wq_raw, wq, wq_in, wq_ready, 0),
                       (wk_raw, wk, wk_in, wk_ready, 0), (wo_raw, wo, wo_in, wv_ready, 1))
            for g in range(2):
                sp.dma_start(acc[:, 4 * g:4 * g + 4, :], x_v[:, 4 * g:4 * g + 4, :]).then_inc(x_in[g], 16)
            for dst, src, s, _, _ in (weights[1], weights[2], weights[0]):
                sp.dma_start(dst[:, :, :], src[0]).then_inc(s, 16)
            for g in range(2, 4):
                sp.dma_start(acc[:, 4 * g:4 * g + 4, :], x_v[:, 4 * g:4 * g + 4, :]).then_inc(x_in[g], 16)
            sp.dma_start(bias_s[:, :], bias.partition_broadcast(P)).then_inc(small_in, 16)
            sp.dma_start(gamma_s[:, :], gamma).then_inc(small_in, 16)
            sp.dma_start(beta_s[:, :], beta).then_inc(small_in, 16)
            sp.wait_ge(wv_ready, 1)
            sp.dma_start(wo_raw[:, :, :], wo[0]).then_inc(wo_in, 16)
            with sp.Fori(1, PAIRS) as it:
                for dst, src, s, split, more in weights:
                    sp.wait_ge(split, it + more)
                    sp.dma_start(dst[:, :, :], src[bass.ds(it, 1)].rearrange("a p k n -> p (a k) n")).then_inc(s, 16)
            sp.wait_ge(wq_ready, PAIRS)
            sp.dma_start(wf_raw, wf).then_inc(wf_in, 16)
            for (g, c), jobs in sorted(ffn_job.items(), key=lambda f: f[1]):
                sp.wait_ge(job_taken, jobs)
                tiles = slice(4 * g + 2 * c, 4 * g + 2 * c + 2)
                sp.dma_start(out_v[:, tiles, :], acc[:, tiles, :]).then_inc(stored, 16)
            sp.wait_ge(stored, 16 * (NT // 2))

        @block.gpsimd
        def _(pool):
            pool.memset(zero[:, :], 0.0).then_inc(const_ready, 1)
            pool.memset(ident[:, :], 0.0).then_inc(const_ready, 1)
            pool.memset(mask[:, :], 0.0).then_inc(const_ready, 1)
            pool.wait_ge(const_ready, 3)
            pool.affine_select(out=ident[:, :], in_=ident[:, :], compare_op=ALU.not_equal, fill=1.0, base=0,
                               pattern=[[-1, P]], channel_multiplier=1).then_inc(const_ready, 1)
            pool.affine_select(out=mask[:, :], in_=mask[:, :], compare_op=ALU.is_ge, fill=MASKED, base=0,
                               pattern=[[-1, P]], channel_multiplier=1).then_inc(const_ready, 1)
            pool.wait_ge(const_ready, 4)
            pool.tensor_copy(ident_b[:, :], ident[:, :]).then_inc(const_ready, 1)

            def split(raw, parts, loaded, ready, it, n):
                pool.wait_ge(loaded, it * 16 + 16)
                pool.tensor_tensor(parts[:, HI], raw[:, :, :], zero[:, :].unsqueeze(2).broadcast_to(raw.shape),
                                   ALU.add).then_inc(hi_done, 1)
                pool.wait_ge(hi_done, n + 1)
                pool.tensor_tensor(parts[:, LO], raw[:, :, :], f32(parts[:, HI]), ALU.subtract).then_inc(ready, 1)

            split(wq_raw, wq_s, wq_in, wq_ready, 0, 0)
            split(wk_raw, wk_s, wk_in, wk_ready, 0, 1)
            split(wv_raw, wv_s, wv_in, wv_ready, 0, 2)

            def pair(it, last):
                jobs = before(it, jobs_in)
                if not is_first(it):
                    pool.wait_ge(job_done, jobs + job_at(it, 0, ("o", 3)))
                split(wo_raw, wo_s, wo_in, wo_ready, it, it * 4 + 3)
                if not last:
                    pool.wait_ge(job_done, jobs + job_at(it, 1, ("v", 1)))
                    split(wv_raw, wv_s, wv_in, wv_ready, it + 1, it * 4 + 4)
                    pool.wait_ge(job_done, jobs + job_at(it, 2, ("qk", 1)))
                    split(wq_raw, wq_s, wq_in, wq_ready, it + 1, it * 4 + 5)
                    pool.wait_ge(job_done, jobs + job_at(it, 2, ("qk", 3)))
                    split(wk_raw, wk_s, wk_in, wk_ready, it + 1, it * 4 + 6)

            pair(0, False)
            with pool.Fori(1, LAST) as it:
                pair(it, False)
            pair(LAST, True)
            pool.wait_ge(job_taken, before(LAST, jobs_in) + job_at(LAST, UNITS - 2, ("bw", 0)))
            for g in range(4):
                pool.wait_ge(norm_ready, 4 + g + 1)
                for n in range(4 * g, 4 * g + 4):
                    pool.tensor_tensor(acc[:, n, :], acc[:, n, :], bias_s[:, :], ALU.add).then_inc(resid_ready, 1)

        @block.tensor
        def _(pe):
            def turn_norm(g, kd, ready, dst):
                pe.wait_ge(norm_ready, ready)
                for j in range(4):
                    mm = pe.transpose(dst[:, j * P:(j + 1) * P], norm[:, j, kd * P:(kd + 1) * P], ident[:, :])
                return mm

            def project_qk(part, k, dst):
                w_s = wq_s if part < 2 else wk_s
                b, hh, c = k // 2, k % 2, part % 2
                cols = slice(b * S + c * BANK, b * S + (c + 1) * BANK)
                for i, (kd, (a, m)) in enumerate([(kd, p) for kd in range(KD) for p in PASSES]):
                    mm = pe.matmul(dst, w_s[:, a, kd, hh * E:(hh + 1) * E], xT[:, m, kd, cols],
                                   start=(i == 0), stop=(i == 3 * KD - 1))
                return mm

            def project_v(c, b, dst):
                for j in range(2):
                    tok = b * S + (2 * c + j) * P
                    for i, (kd, (a, m)) in enumerate([(kd, p) for kd in range(KD) for p in PASSES]):
                        mm = pe.matmul(dst[:, j * 2 * E:(j + 1) * 2 * E], xT[:, a, kd, tok:tok + P], wv_s[:, m, kd, :],
                                       start=(j == 0 and i == 0), stop=(i == 3 * KD - 1), skip_group_check=True)
                return mm

            def weighted_v(half, k, dst, keys):
                b, hh = k // 2, k % 2
                pT = pT1 if half else pT0
                n_keys = HALF * (half + 1)
                for j in keys:
                    lo = min(max(0, j - half * HALF) * P, BANK - 2 * P)
                    for i, (a, m) in enumerate(PASSES):
                        mm = pe.matmul(dst[:, lo:BANK], v[:, b, a, j, hh * E:(hh + 1) * E], pT[:, m, j, lo:BANK],
                                       start=(j == 0 and i == 0), stop=(j == n_keys - 1 and i == 2))
                return mm

            def project_o(c, hh, dst):
                for j in range(2):
                    tok = (2 * c + j) * P
                    for i, (a, m) in enumerate(PASSES):
                        mm = pe.matmul(dst[:, j * D:(j + 1) * D], zT[:, a, tok:tok + P], wo_s[:, m, hh, :],
                                       start=(j == 0 and i == 0), stop=(i == 2), skip_group_check=True)
                return mm

            def project_ffn(g, c, dst):
                for j in range(2):
                    tok = (4 * g + 2 * c + j) * P
                    for i, (kd, a) in enumerate([(kd, a) for kd in range(KD) for a in (LO, HI)]):
                        mm = pe.matmul(dst[:, j * D:(j + 1) * D], xT[:, a, kd, tok:tok + P], wf_s[:, kd, :],
                                       start=(j == 0 and i == 0), stop=(i == 3), skip_group_check=True)
                return mm

            def score_tile(k, t):
                par = k % 2
                width = max(2, t + 1 + (t == 4)) * P
                for c in range(0, width, BANK):
                    n = min(BANK, width - c)
                    diagonal = c <= t * P < c + n
                    for i, (a, m) in enumerate(PASSES):
                        mm = pe.matmul(scores[:, t % 2, c:c + n], qT[:, par, a, t * P:(t + 1) * P], kT[:, par, m, c:c + n],
                                       start=(i == 0), stop=(i == 2 and not diagonal))
                    if diagonal:
                        mm = pe.matmul(scores[:, t % 2, t * P:(t + 1) * P], ident_b[:, :], mask[:, :], start=False, stop=True)
                mm.then_inc(scores_ready, 1)

            def turn_tile(t, g, g0):
                for n in range(banks(t)):
                    if not isinstance(g0, int) or g0 + g + n >= 2:
                        pe.wait_ge(plo_ready, g0 + (g + n - 1))
                    for j in range(4 * n, min(4 * n + 4, t + 1)):
                        mm = pe.transpose(turned[:, (g + n) % 2, (j % 4) * P:(j % 4 + 1) * P],
                                          probs[:, t % 2, j * P:(j + 1) * P], ident[:, :])
                    mm.then_inc(turned_ready, 1)

            def run(item, n, jobs, parity, it, k, groups):
                kind, arg = item
                if kind in NO_JOB and kind != "pv_part":
                    return n
                dst = ring[:, (parity + n) % 2, :]
                if (kind, arg) == ("pv", 1):
                    pass
                elif not isinstance(jobs, int) or jobs + n >= 2:
                    pe.wait_ge(job_taken, jobs + (n - 1))
                if kind == "x":
                    mm = turn_norm(*arg, arg[0] + 1, dst)
                elif kind == "xf":
                    mm = turn_norm(*arg, 4 + arg[0] + 1, dst)
                elif kind == "qk":
                    if k is None:
                        pe.wait_ge(job_taken, 2 if arg in (0, 2) else 6)
                        pe.wait_ge(wk_ready if arg >= 2 else wq_ready, 1)
                    elif k == UNITS - 1 and arg in (0, 2):
                        pe.wait_ge(wk_ready if arg else wq_ready, it + 2)
                    mm = project_qk(arg, 0 if k is None else (k + 1) % UNITS, dst)
                elif kind == "v":
                    if k is None:
                        pe.wait_ge(wv_ready, 1)
                        mm = project_v(arg, 0, dst)
                    else:
                        if is_first(it) and k == 0 and arg == 0:
                            pe.wait_ge(job_taken, jobs + job_at(it, 0, ("x", (3, 1))))
                        if k == 2 and arg == 0:
                            pe.wait_ge(wv_ready, it + 2)
                        mm = project_v(arg + 2 * (k % 2), (k // 2 + 1) % 2, dst)
                elif kind == "pv" and arg == 0:
                    pe.wait_ge(plo_ready, groups + (k * GROUPS + HALF))
                    mm = weighted_v(0, k, dst, range(HALF))
                elif kind == "pv_part":
                    pe.wait_ge(plo_ready, groups + (k * GROUPS - 1))
                    weighted_v(1, (k - 1) % UNITS, dst, range(HALF))
                    return n
                elif kind == "pv":
                    pe.wait_ge(plo_ready, groups + k * GROUPS)
                    mm = weighted_v(1, (k - 1) % UNITS, dst, range(HALF, QT))
                elif kind == "o":
                    if k == 1 and arg == 0:
                        pe.wait_ge(wo_ready, it + 1)
                    if arg == 0 and k > 0:
                        pe.wait_ge(job_taken, jobs + job_at(it, k - 1, ("pv", 0)))
                    elif arg == 0:
                        pe.wait_ge(job_taken, jobs - (jobs_in(flat(UNIT)) - job_at(1, 0, ("pv", 0))))
                    elif arg == 2:
                        pe.wait_ge(job_taken, jobs + job_at(it, k, ("pv", 1)) if k < UNITS else last_pv)
                    mm = project_o(arg, (k - 1) % 2, dst)
                elif kind == "o_own":
                    pe.wait_ge(job_taken, jobs + job_at(it, k, ("pv", 0)))
                    mm = project_o(arg, k % 2, dst)
                elif kind == "wsum":
                    pe.wait_ge(wabs_ready, 1)
                    mm = pe.matmul(dst[:, 0:1], one[:, :].broadcast_to([P, P]), wabs[:, :], start=True, stop=True)
                elif kind == "bw":
                    pe.wait_ge(wf_ready, 1)
                    pe.wait_ge(small_in, 48)
                    for kd in range(KD):
                        mm = pe.matmul(dst[:, 0:D], beta_s[:, kd:kd + 1].broadcast_to([P, P]), f32(wf_s[:, kd, :]),
                                       start=(kd == 0), stop=(kd == KD - 1))
                else:
                    pe.wait_ge(job_taken, xf_jobs[arg[0]])
                    mm = project_ffn(*arg, dst)
                mm.then_inc(job_done, 1)
                if kind == "xf" and arg[1] == KD - 1:
                    xf_jobs[arg[0]] = jobs + n + 1
                return n + 1

            xf_jobs = {}

            pe.wait_ge(const_ready, 6)
            n = 0
            for item in PROLOGUE:
                n = run(item, n, 0, 0, 0, None, 0)
            pe.wait_ge(job_taken, 8)
            score_tile(0, 0)

            def pair(it, last):
                jobs, groups, tiles = before(it, jobs_in), it * (UNITS * GROUPS), it * (UNITS * QT)
                n, g = 0, 0
                for k in range(UNITS):
                    for t, slot in enumerate(plan(it, k)):
                        for item in slot:
                            if item != NEXT:
                                n = run(item, n, jobs, odd(it), it, k, groups)
                            elif t < QT - 1:
                                score_tile(k, t + 1)
                            elif not last or k < UNITS - 1:
                                pe.wait_ge(job_taken, jobs + job_at(it, k, ("qk", 3)))
                                score_tile((k + 1) % UNITS, 0)
                        pe.wait_ge(probs_ready, tiles + (k * QT + t + 1))
                        turn_tile(t, g, groups)
                        g += banks(t)
                return jobs, n

            pair(0, False)
            with pe.Fori(1, LAST) as it:
                pair(it, False)
            jobs, n = pair(LAST, True)
            last_pv = jobs + n + 1
            for item in EPILOGUE:
                n = run(item, n, jobs, odd(LAST), LAST, UNITS, LAST * UNITS * GROUPS)

        @block.scalar
        def _(act):
            def exp_tile(k, t, tile):
                act.wait_ge(max_ready, tile + 1)
                act.activation(probs[:, t % 2, 0:(t + 1) * P], scores[:, t % 2, 0:(t + 1) * P], ACT.Exp,
                               bias=negmax[:, t % 2:t % 2 + 1],
                               accum_out=rowsum[:, k % 2, t:t + 1]).then_inc(probs_ready, 1)

            def turned_hi(t, g, g0):
                pT = pT1 if t >= HALF else pT0
                q = (t % HALF) * P
                for n in range(banks(t)):
                    act.wait_ge(turned_ready, g0 + (g + n + 1))
                    w = min(4, t + 1 - 4 * n)
                    act.activation(pT[:, HI, 4 * n:4 * n + w, q:q + P],
                                   turned[:, (g + n) % 2, 0:w * P].rearrange("p (j q) -> p j q", q=P),
                                   ACT.Copy).then_inc(phi_ready, 1)

            lns = [0]

            def run(item, n, jobs, parity, k):
                kind, arg = item
                if kind in NO_JOB:
                    if kind == "stats":
                        lns[0] += 2
                    elif kind == "rstd":
                        g, m = arg
                        act.wait_ge(ln_step, lns[0])
                        variance = mv[:, 4 * g:4 * (g + m), 1]
                        if k is None:
                            ins = act.activation(std[:, 4 * g:4 * (g + m)], variance, ACT.Sqrt, bias=eps[:, 0:1])
                        else:
                            ins = act.activation(std[:, 4 * g:4 * (g + m)], variance, ACT.Sqrt, bias=eps[:, 1:2],
                                                 scale=1.0 + LN_EPS)
                        ins.then_inc(std_ready, 1)
                        lns[0] += 1
                    return n
                if kind in NO_SPLIT:
                    return n + 1
                src, scale = ring[:, (parity + n) % 2, :], 1.0
                if kind in ("x", "xf"):
                    g, kd = arg
                    dst = xT[:, HI, kd, 4 * g * P:(4 * g + 4) * P]
                    if kind == "xf":
                        scale = gamma_s[:, kd:kd + 1]
                elif kind == "qk":
                    k_next = 0 if k is None else (k + 1) % 2
                    dst = (qT if arg < 2 else kT)[:, k_next, HI, (arg % 2) * BANK:(arg % 2 + 1) * BANK]
                    scale = SCALE if arg < 2 else 1.0
                elif kind == "v":
                    c, b = (arg, 0) if k is None else (arg + 2 * (k % 2), (k // 2 + 1) % 2)
                    dst = v[:, b, HI, 2 * c:2 * c + 2, :].rearrange("p a n -> p (a n)")
                else:
                    dst = zT[:, HI, arg * BANK:(arg + 1) * BANK]
                act.wait_ge(job_done, jobs + (n + 1))
                act.activation(dst, src, ACT.Copy, scale=scale).then_inc(jhi_ready, 1)
                return n + 1

            act.wait_ge(dve_const, 1)
            pro = 0
            for item in PROLOGUE:
                pro = run(item, pro, 0, 0, None)
            exp_tile(0, 0, 0)

            def pair(it, last):
                jobs, groups, tiles = before(it, jobs_in), it * (UNITS * GROUPS), it * (UNITS * QT)
                n, g = 0, 0
                for k in range(UNITS):
                    for t, slot in enumerate(plan(it, k)):
                        for item in slot:
                            if item != NEXT:
                                n = run(item, n, jobs, odd(it), k)
                            elif t < QT - 1:
                                exp_tile(k, t + 1, tiles + (k * QT + t + 1))
                            elif not last or k < UNITS - 1:
                                exp_tile((k + 1) % UNITS, 0, tiles + (k + 1) * QT)
                        turned_hi(t, g, groups)
                        g += banks(t)
                return jobs, n

            pair(0, False)
            with act.Fori(1, LAST) as it:
                pair(it, False)
            jobs, n = pair(LAST, True)
            for item in EPILOGUE:
                n = run(item, n, jobs, odd(LAST), UNITS)

        @block.vector
        def _(dve):
            dve.memset(eps[:, 0:1], LN_EPS)
            dve.memset(eps[:, 1:2], LN_EPS * LN_EPS).then_inc(dve_const, 1)
            for a in (HI, LO):
                dve.memset(f32(pT0[:, a, HALF - 1, BANK - 2 * P:BANK - P]), 0.0)
                dve.memset(f32(pT1[:, a, QT - 1, BANK - 2 * P:BANK - P]), 0.0)
            dve.memset(one[:, :], 1.0)

            def max_tile(t, tile):
                dve.wait_ge(scores_ready, tile + 1)
                dve.tensor_reduce(negmax[:, t % 2:t % 2 + 1], scores[:, t % 2, 0:(t + 1) * P], AX_X, ALU.max,
                                  negate=True).then_inc(max_ready, 1)

            def invert_sums(k, units):
                dve.wait_ge(probs_ready, units * QT)
                dve.reciprocal(inv[:, k % 2, :], rowsum[:, k % 2, :]).then_inc(inv_ready, 1)

            def turned_lo(t, g, g0):
                pT = pT1 if t >= HALF else pT0
                q = (t % HALF) * P
                for n in range(banks(t)):
                    dve.wait_ge(phi_ready, g0 + (g + n + 1))
                    w = min(4, t + 1 - 4 * n)
                    dve.tensor_tensor(pT[:, LO, 4 * n:4 * n + w, q:q + P],
                                      turned[:, (g + n) % 2, 0:w * P].rearrange("p (j q) -> p j q", q=P),
                                      f32(pT[:, HI, 4 * n:4 * n + w, q:q + P]), ALU.subtract).then_inc(plo_ready, 1)

            def add_o(c, k, src):
                for j in range(2):
                    t = 2 * c + j
                    tile = acc[:, (k // 2) * QT + t, :]
                    last = dve.scalar_tensor_tensor(out=tile, in0=src[:, j * D:(j + 1) * D],
                                                    scalar=inv[:, k % 2, t:t + 1], in1=tile,
                                                    op0=ALU.mult, op1=ALU.add)
                return last

            def ternary_threshold(src):
                return dve.tensor_scalar(thr[:, 0:1], src[:, 0:1], 0.5 / (D * D), 0.5 * Q_EPS, ALU.mult, ALU.add)

            def ternary_weight():
                dve.tensor_scalar(thr[:, 1:2], thr[:, 0:1], -1.0, None, ALU.mult).then_inc(tern_step, 1)
                dve.wait_ge(tern_step, 1)
                dve.tensor_scalar(wf_neg, wf_raw, thr[:, 1:2], None, ALU.is_lt).then_inc(tern_step, 1)
                dve.wait_ge(tern_step, 2)
                dve.scalar_tensor_tensor(out=wf_s[:, :, :], in0=wf_raw, scalar=thr[:, 0:1], in1=wf_neg,
                                         op0=ALU.is_gt, op1=ALU.subtract).then_inc(wf_ready, 1)

            lns = [0]
            stds = [0]

            def layernorm_item(kind, arg):
                if kind == "stats":
                    for j in range(4):
                        last = dve.bn_stats(stats[:, 4 * arg + j, :], acc[:, 4 * arg + j, :])
                    last.then_inc(ln_step, 1)
                    dve.wait_ge(ln_step, lns[0] + 1)
                    for j in range(4):
                        last = dve.bn_aggr(mv[:, 4 * arg + j, :], stats[:, 4 * arg + j, :])
                    last.then_inc(ln_step, 1)
                    lns[0] += 2
                elif kind == "rstd":
                    g, m = arg
                    stds[0] += 1
                    dve.wait_ge(std_ready, stds[0])
                    dve.reciprocal(rstd[:, 4 * g:4 * (g + m)], std[:, 4 * g:4 * (g + m)]).then_inc(ln_step, 1)
                    lns[0] += 1
                    dve.wait_ge(ln_step, lns[0])
                else:
                    for j in range(4):
                        t = 4 * arg + j
                        last = dve.tensor_scalar(norm[:, j, :], acc[:, t, :], mv[:, t, 0:1], rstd[:, t:t + 1],
                                                 ALU.subtract, ALU.mult)
                    last.then_inc(norm_ready, 1)

            def run(item, n, s, jobs, splits, parity, it, k):
                kind, arg = item
                if kind == "wabs":
                    dve.wait_ge(wf_in, 16)
                    dve.tensor_reduce(wabs[:, :], wf_raw, AX_XY, ALU.add, apply_absolute_value=True).then_inc(wabs_ready, 1)
                    return n, s
                if kind == "pv_part":
                    return n, s
                if kind in NO_JOB:
                    if kind == "stats" and k is not None:
                        dve.wait_ge(job_taken, jobs + n)
                    layernorm_item(kind, arg)
                    return n, s
                src = ring[:, (parity + n) % 2, :]
                if kind in NO_SPLIT:
                    if kind == "o" and arg == 0:
                        dve.wait_ge(inv_ready, it * UNITS + k)
                    dve.wait_ge(job_done, jobs + (n + 1))
                    if kind == "o":
                        add_o(arg, (k - 1) % UNITS, src).then_inc(job_taken, 1)
                    elif kind == "o_own":
                        add_o(arg, k, src).then_inc(job_taken, 1)
                    elif kind == "wsum":
                        ternary_threshold(src).then_inc(job_taken, 1)
                        dve.wait_ge(job_taken, jobs + (n + 1))
                        ternary_weight()
                    elif kind == "bw":
                        dve.wait_ge(small_in, 48)
                        dve.tensor_tensor(bias_s[:, :], src[:, 0:D], bias_s[:, :], ALU.add).then_inc(job_taken, 1)
                    else:
                        g, c = arg
                        tiles = acc[:, 4 * g + 2 * c:4 * g + 2 * c + 2, :].rearrange("p n d -> p (n d)")
                        dve.wait_ge(resid_ready, 4 * g + 2 * c + 2)
                        dve.tensor_tensor(tiles, src, tiles, ALU.add).then_inc(job_taken, 1)
                    return n + 1, s
                scale = None
                if kind in ("x", "xf"):
                    g, kd = arg
                    hi, lo = (xT[:, a, kd, 4 * g * P:(4 * g + 4) * P] for a in (HI, LO))
                    if kind == "xf":
                        scale = gamma_s[:, kd:kd + 1]
                elif kind == "qk":
                    k_next = 0 if k is None else (k + 1) % 2
                    hi, lo = ((qT if arg < 2 else kT)[:, k_next, a, (arg % 2) * BANK:(arg % 2 + 1) * BANK] for a in (HI, LO))
                    scale = SCALE if arg < 2 else None
                elif kind == "v":
                    c, b = (arg, 0) if k is None else (arg + 2 * (k % 2), (k // 2 + 1) % 2)
                    hi, lo = (v[:, b, a, 2 * c:2 * c + 2, :].rearrange("p a n -> p (a n)") for a in (HI, LO))
                else:
                    hi, lo = (zT[:, a, arg * BANK:(arg + 1) * BANK] for a in (HI, LO))
                dve.wait_ge(jhi_ready, splits + (s + 1))
                if scale is None:
                    ins = dve.tensor_tensor(lo, src, f32(hi), ALU.subtract)
                else:
                    ins = dve.scalar_tensor_tensor(out=lo, in0=src, scalar=scale, in1=f32(hi),
                                                   op0=ALU.mult, op1=ALU.subtract)
                ins.then_inc(job_taken, 1)
                return n + 1, s + 1

            n, s = 0, 0
            for item in PROLOGUE:
                if item[0] == "stats":
                    dve.wait_ge(x_in[item[1]], 16)
                n, s = run(item, n, s, 0, 0, 0, 0, None)
            max_tile(0, 0)

            def pair(it, last):
                jobs, splits = before(it, jobs_in), before(it, splits_in)
                groups, tiles = it * (UNITS * GROUPS), it * (UNITS * QT)
                n, s, g = 0, 0, 0
                for k in range(UNITS):
                    for t, slot in enumerate(plan(it, k)):
                        if t == 0 and has_previous(it, k):
                            invert_sums((k - 1) % UNITS, it * UNITS + k)
                        if last and k == UNITS - 1 and t == QT - 1:
                            invert_sums(k, PAIRS * UNITS)
                            dve.wait_ge(inv_ready, PAIRS * UNITS)
                        for item in slot:
                            if item != NEXT:
                                n, s = run(item, n, s, jobs, splits, odd(it), it, k)
                            elif t < QT - 1:
                                max_tile(t + 1, tiles + (k * QT + t + 1))
                            elif not last or k < UNITS - 1:
                                max_tile(0, tiles + (k + 1) * QT)
                        turned_lo(t, g, groups)
                        g += banks(t)
                return jobs, splits, n, s

            pair(0, False)
            with dve.Fori(1, LAST) as it:
                pair(it, False)
            jobs, splits, n, s = pair(LAST, True)
            for item in EPILOGUE:
                n, s = run(item, n, s, jobs, splits, odd(LAST), LAST, UNITS)

_INS = ("x", "wq", "wk", "wv", "wo", "wf", "gamma", "beta", "bias")


def kernel(L0_attn_x, L0_attn_W_Q, L0_attn_W_K, L0_attn_W_V, L0_attn_W_O, L0_ffn_weight, L0_ffn_bias,
           L0_ffn_ln_gamma, L0_ffn_ln_beta):
    import numpy as np
    import concourse.bacc as bacc
    from concourse.bass_utils import run_bass_kernel_spmd as run

    B, S, D = L0_attn_x.shape
    H, E, _ = L0_attn_W_Q.shape

    def in_weight(w):
        return np.ascontiguousarray(np.asarray(w).reshape(H // 2, 2, E, D // P, P).transpose(0, 4, 3, 1, 2)
                                    .reshape(H // 2, P, D // P, 2 * E))

    host = {
        "x": np.asarray(L0_attn_x).reshape(B * S, D),
        "wq": in_weight(L0_attn_W_Q),
        "wk": in_weight(L0_attn_W_K),
        "wv": in_weight(L0_attn_W_V),
        "wo": np.ascontiguousarray(np.asarray(L0_attn_W_O).reshape(H // 2, 2, D, E).transpose(0, 3, 1, 2)),
        "wf": np.ascontiguousarray(np.asarray(L0_ffn_weight).reshape(D, D // P, P).transpose(2, 1, 0)),
        "gamma": np.ascontiguousarray(np.asarray(L0_ffn_ln_gamma).reshape(D // P, P).T),
        "beta": np.ascontiguousarray(np.asarray(L0_ffn_ln_beta).reshape(D // P, P).T),
        "bias": np.asarray(L0_ffn_bias),
    }
    nc = bacc.Bacc("TRN2", target_bir_lowering=False, num_devices=1)
    args = [nc.dram_tensor(f"in_{n}", host[n].shape, mybir.dt.from_np(host[n].dtype), kind="ExternalInput").ap()
            for n in _INS]
    out = nc.dram_tensor("out", (B * S, D), F32, kind="ExternalOutput").ap()
    attention_ffn(nc, *args, out)
    r = run(nc, [{f"in_{n}": host[n] for n in _INS}], core_ids=[0])
    return r.results[0]["out"].reshape(B, S, D)
```

```python
from contextlib import ExitStack

import concourse.bass as bass
from concourse import mybir

F32 = mybir.dt.float32
F32R = mybir.dt.float32r
BF16 = mybir.dt.bfloat16
ALU = mybir.AluOpType
ACT = mybir.ActivationFunctionType
AX_X = mybir.AxisListType.X
AX_XY = mybir.AxisListType.XY

P = 128
BANK = 512
WARM_UP = 48
LN_EPS = 1e-5
Q_EPS = 1e-5
MASKED = -1e30

HI, LO = 0, 1
PASSES = ((HI, LO), (LO, HI), (HI, HI))

NO_JOB = ("stats", "rstd", "norm", "inv", "wabs", "next", "turn", "pv_part")
NEXT, TURN = ("next", 0), ("turn", 0)
NO_SPLIT = ("o", "o_own", "wsum", "bw", "ff")
PROLOGUE = (
    ("stats", (0, 4)), ("rstd", (0, 4)), ("norm", (0, 4)), ("stats", (4, 4)), ("rstd", (4, 4)),
    ("x", (0, 4, 0)), ("x", (0, 4, 1)), ("norm", (4, 4)), ("stats", (8, 8)), ("qk0", 0), ("rstd", (8, 8)),
    ("qk0", 2),
)
UNIT = (
    (("qk", 0), NEXT),
    (("pv_part", 1), NEXT),
    (("pv", 1), ("o", 0), NEXT),
    (("qk", 2), NEXT),
    (("o", 1), ("qk", 1), NEXT),
    (NEXT, ("o", 2)),
    (("v", 0), ("qk", 3), NEXT, ("o", 3), ("v", 1)),
    (NEXT, ("pv", 0)),
)
UNIT_SCALAR = (
    (NEXT, ("qk", 0)),
    (NEXT,),
    (("pv", 1), NEXT, ("o", 0)),
    (("qk", 2), ("o", 1), NEXT),
    (("qk", 1), TURN, NEXT),
    (("o", 2), TURN, NEXT),
    (("v", 0), ("qk", 3), ("o", 3), NEXT, ("v", 1)),
    (("pv", 0), NEXT),
)
UNIT_VECTOR = (
    (NEXT, ("qk", 0)),
    (NEXT,),
    (("pv", 1), NEXT, ("o", 0)),
    (("qk", 2), NEXT, ("o", 1)),
    (NEXT, ("qk", 1)),
    (NEXT, ("o", 2)),
    (("v", 0), ("qk", 3), NEXT, ("o", 3), ("v", 1)),
    (NEXT, ("pv", 0)),
)
FIRST_UNIT = (
    (NEXT, ("x", (4, 4, 0)), ("x", (4, 4, 1))),
    (NEXT, ("norm", (8, 4)), ("qk0", 3), TURN, ("qk0", 1)),
    (NEXT, ("v0", 0), TURN, ("x", (8, 4, 0)), ("v0", 1), ("x", (8, 4, 1))),
    (("norm", (12, 4)), ("v0", 2), TURN, NEXT),
    (NEXT, ("x", (12, 4, 0)), ("v0", 3), TURN, ("x", (12, 4, 1)), ("pv", 0)),
    (("qk", 0), NEXT, ("qk", 2)),
    (("qk", 1), NEXT, ("qk", 3)),
    (("v", 0), NEXT, ("v", 1)),
)
LAST_BUT_ONE = (
    (NEXT, ("qk", 0), ("wabs", 0)),
    (NEXT, ("pv_part", 1)),
    (("pv", 1), NEXT, ("o", 0)),
    (("qk", 2), NEXT, ("o", 1), TURN, ("o", 2)),
    (("qk", 1), NEXT, ("o", 3)),
    (("wsum", 0), NEXT, ("stats", (0, 4)), ("qk", 3)),
    (NEXT, ("bw", 0), ("stats", (4, 4)), ("rstd", (0, 8)), ("norm", (0, 4))),
    (NEXT, ("pv", 0), ("xf", (0, 4, 0))),
)
LAST_UNIT = (
    (NEXT, ("xf", (0, 4, 1)), ("norm", (4, 4))),
    (("pv_part", 1), NEXT),
    (("pv", 1), NEXT, ("ff", 0), ("o", 0)),
    (NEXT, ("o", 1), ("o", 2), ("o", 3), ("ff", 1)),
    (NEXT, ("xf", (4, 4, 0)), ("xf", (4, 4, 1))),
    (NEXT, ("pv", 0), ("ff", 2)),
    (NEXT, ("inv", (0, 6)), ("o_own", 0), ("o_own", 1)),
    (NEXT, ("pv_q", 2), ("ff", 3), ("o_own", 2)),
)
EPILOGUE = (
    ("stats", (8, 6)), ("inv", (6, 2)), ("rstd", (8, 6)), ("pv_q", 3), ("norm", (8, 4)), ("xf", (8, 4, 0)),
    ("xf", (8, 4, 1)), ("norm", (12, 2)), ("o_own", 3), ("ff", 4), ("stats", (14, 2)), ("xf", (12, 2, 0)),
    ("xf", (12, 2, 1)), ("rstd", (14, 2)), ("norm", (14, 2)), ("ff", 5), ("ff", 6), ("xf", (14, 2, 0)),
    ("xf", (14, 2, 1)), ("ff", 7),
)


def jobs_in(items):
    return sum(kind not in NO_JOB for kind, _ in items)


def splits_in(items):
    return sum(kind not in NO_JOB + NO_SPLIT for kind, _ in items)


def in_full(slot):
    return slot if TURN in slot else slot + (TURN,)


def flat(unit):
    return [item for slot in unit for item in slot]


def attention_ffn(nc, x, wq, wk, wv, wo, wf, gamma, beta, bias, out):
    TOK, D = x.shape
    PAIRS = wq.shape[0]
    B = 2
    S = TOK // B
    E = P
    KD = D // P
    NT = TOK // P
    QT = S // P
    HALF = QT // 2
    UNITS = 2 * B
    LAST = PAIRS - 1
    SCALE = float(E) ** -0.5
    assert (D, E, QT, KD, S) == (256, P, 8, 2, 2 * BANK)

    x_v = x.rearrange("(n p) d -> p n d", p=P)
    out_v = out.rearrange("(n p) d -> p n d", p=P)

    def banks(t):
        return -(-(t + 1) // 4)

    GROUPS = sum(banks(t) for t in range(QT))

    def first_column(t):
        return P if t == BANK // P else 0

    def score_columns(t):
        return slice(first_column(t), first_column(t) + (t + 1) * P)

    def is_first(it):
        return isinstance(it, int) and it == 0

    def plan(it, k, unit=UNIT):
        if is_first(it) and k == 0:
            return FIRST_UNIT
        if isinstance(it, int) and it == LAST and k >= UNITS - 2:
            return (LAST_BUT_ONE, LAST_UNIT)[k - (UNITS - 2)]
        return unit

    def before(it, count):
        if is_first(it):
            return count(PROLOGUE)
        return it * (UNITS * count(flat(UNIT))) + (count(PROLOGUE) + count(flat(FIRST_UNIT)) - count(flat(UNIT)))

    def odd(it):
        return jobs_in(PROLOGUE) % 2 if is_first(it) else before(1, jobs_in) % 2

    for unit in (UNIT_SCALAR, UNIT_VECTOR):
        assert [i for i in flat(unit) if i[0] not in NO_JOB] == [i for i in flat(UNIT) if i[0] not in NO_JOB]
    assert UNITS * jobs_in(flat(UNIT)) % 2 == 0 and GROUPS % 2 == 0

    def job_at(it, k, item):
        n = 0
        for u in range(k + 1):
            for i in flat(plan(it, u)):
                n += i[0] not in NO_JOB
                if u == k and i == item:
                    return n
        raise AssertionError(item)

    def first_job(*item):
        items = list(PROLOGUE) + flat(FIRST_UNIT)
        return jobs_in(items[:items.index(item) + 1])

    with ExitStack() as ctx:
        def sb(name, shape, dt):
            return ctx.enter_context(nc.sbuf_tensor(name, shape, dt))

        def pb(name, shape, dt):
            return ctx.enter_context(nc.psum_tensor(name, shape, dt))

        def sem(name):
            return ctx.enter_context(nc.semaphore(name))

        scores = pb("scores", [P, 2, 2 * BANK], F32)
        turned = pb("turned", [P, 2, BANK], F32)
        ring = pb("ring", [P, 2, BANK], F32)

        xT = sb("xT", [P, 2, KD, TOK], F32R)
        qT = sb("qT", [P, 2, 2, S], F32R)
        kT = sb("kT", [P, 2, 2, S], F32R)
        v = sb("v", [P, B, 2, QT, 2 * E], F32R)
        pT0 = sb("pT0", [P, 2, HALF, BANK], F32R)
        pT1 = sb("pT1", [P, 2, QT, BANK], F32R)
        zT = sb("zT", [P, 2, S], F32R)
        acc = sb("acc", [P, NT, D], F32)
        probs = sb("probs", [P, 2, S], F32)
        norm = sb("norm", [P, 4, D], F32)
        wq_s = sb("wq_s", [P, 2, KD, 2 * E], F32R)
        wk_s = sb("wk_s", [P, 2, KD, 2 * E], F32R)
        wv_s = sb("wv_s", [P, 2, KD, 2 * E], F32R)
        wo_s = sb("wo_s", [P, 2, 2, D], F32R)
        wq_raw = sb("wq_raw", [P, KD, 2 * E], F32)
        wk_raw = sb("wk_raw", [P, KD, 2 * E], F32)
        wv_raw = sb("wv_raw", [P, KD, 2 * E], F32)
        wo_raw = wv_raw
        wf_s = sb("wf_s", [P, KD, D], F32R)
        bias_s = sb("bias_s", [P, D], F32)
        gamma_s = sb("gamma_s", [P, KD], F32)
        beta_s = sb("beta_s", [P, KD], F32)
        ident = sb("ident", [P, P], F32)
        ident_b = sb("ident_b", [P, P], BF16)
        mask = sb("mask", [P, P], BF16)
        one = sb("one", [P, 1], F32)
        zero = sb("zero", [P, 1], F32)
        eps = sb("eps", [P, 2], F32)
        negmax = sb("negmax", [P, 2], F32)
        rowsum = sb("rowsum", [P, 2, QT], F32)
        inv = sb("inv", [P, 2, QT], F32)
        stats = sb("stats", [P, NT, 6], F32)
        mv = sb("mv", [P, NT, 2], F32)
        std = sb("std", [P, NT], F32)
        rstd = sb("rstd", [P, NT], F32)
        wabs = sb("wabs", [P, 1], F32)
        thr = sb("thr", [P, 2], F32)
        unused = sb("unused", [P, 1], F32)

        wf_raw = wq_raw[:, :, 0:D]
        wf_neg = wk_raw[:, :, 0:D]

        x_in = [sem(f"x_in{g}") for g in range(4)]
        small_in = sem("small_in")
        wq_in, wk_in, wv_in, wo_in, wf_in = sem("wq_in"), sem("wk_in"), sem("wv_in"), sem("wo_in"), sem("wf_in")
        wq_ready, wk_ready, wv_ready, wo_ready = sem("wq_ready"), sem("wk_ready"), sem("wv_ready"), sem("wo_ready")
        hi_done = sem("hi_done")
        const_ready = sem("const_ready")
        dve_const = sem("dve_const")
        scores_ready = sem("scores_ready")
        max_ready = sem("max_ready")
        probs_ready = sem("probs_ready")
        turned_ready = sem("turned_ready")
        phi_ready = sem("phi_ready")
        plo_ready = sem("plo_ready")
        job_done = sem("job_done")
        jhi_ready = sem("jhi_ready")
        job_taken = sem("job_taken")
        inv_ready = sem("inv_ready")
        ln_step = sem("ln_step")
        std_ready = sem("std_ready")
        norm_ready = sem("norm_ready")
        wabs_ready = sem("wabs_ready")
        tern_step = sem("tern_step")
        wf_ready = sem("wf_ready")
        resid_ready = sem("resid_ready")
        stored = sem("stored")

        def f32(ap):
            return ap.bitcast(F32)

        ffn_job = {}
        n = before(LAST, jobs_in)
        for item in [i for k in range(UNITS) for i in flat(plan(LAST, k))] + list(EPILOGUE):
            n += item[0] not in NO_JOB
            if item[0] == "ff":
                ffn_job[item[1]] = n

        block = ctx.enter_context(nc.Block())

        @block.sync
        def _(sp):
            weights = ((wv_raw, wv, wv_in, wo_ready, 0), (wq_raw, wq, wq_in, wq_ready, 0),
                       (wk_raw, wk, wk_in, wk_ready, 0), (wo_raw, wo, wo_in, wv_ready, 1))
            wq_load, wk_load, wv_load = weights[1], weights[2], weights[0]
            for g, (dst, src, s, _, _) in enumerate((wq_load, wk_load, wv_load)):
                sp.dma_start(acc[:, 4 * g:4 * g + 4, :], x_v[:, 4 * g:4 * g + 4, :]).then_inc(x_in[g], 16)
                sp.dma_start(dst[:, :, :], src[0]).then_inc(s, 16)
            sp.dma_start(acc[:, 12:16, :], x_v[:, 12:16, :]).then_inc(x_in[3], 16)
            sp.dma_start(bias_s[:, :], bias.partition_broadcast(P)).then_inc(small_in, 16)
            sp.dma_start(gamma_s[:, :], gamma).then_inc(small_in, 16)
            sp.dma_start(beta_s[:, :], beta).then_inc(small_in, 16)
            sp.wait_ge(wv_ready, 1)
            sp.dma_start(wo_raw[:, :, :], wo[0]).then_inc(wo_in, 16)
            with sp.Fori(1, PAIRS) as it:
                for dst, src, s, split, more in weights:
                    sp.wait_ge(split, it + more)
                    sp.dma_start(dst[:, :, :], src[bass.ds(it, 1)].rearrange("a p k n -> p (a k) n")).then_inc(s, 16)
            sp.wait_ge(wq_ready, PAIRS)
            sp.dma_start(wf_raw, wf).then_inc(wf_in, 16)
            for c, jobs in ffn_job.items():
                sp.wait_ge(job_taken, jobs)
                tiles = slice(2 * c, 2 * c + 2)
                sp.dma_start(out_v[:, tiles, :], acc[:, tiles, :]).then_inc(stored, 16)
            sp.wait_ge(stored, 16 * (NT // 2))

        @block.gpsimd
        def _(pool):
            pool.memset(zero[:, :], 0.0).then_inc(const_ready, 1)
            pool.memset(ident[:, :], 0.0).then_inc(const_ready, 1)
            pool.memset(mask[:, :], 0.0).then_inc(const_ready, 1)
            pool.wait_ge(const_ready, 3)
            pool.affine_select(out=ident[:, :], in_=ident[:, :], compare_op=ALU.not_equal, fill=1.0, base=0,
                               pattern=[[-1, P]], channel_multiplier=1).then_inc(const_ready, 1)
            pool.affine_select(out=mask[:, :], in_=mask[:, :], compare_op=ALU.is_ge, fill=MASKED, base=0,
                               pattern=[[-1, P]], channel_multiplier=1).then_inc(const_ready, 1)
            pool.wait_ge(const_ready, 4)
            pool.tensor_copy(ident_b[:, :], ident[:, :]).then_inc(const_ready, 1)

            def split(raw, parts, loaded, ready, it, n):
                pool.wait_ge(loaded, it * 16 + 16)
                pool.tensor_tensor(parts[:, HI], raw[:, :, :], zero[:, :].unsqueeze(2).broadcast_to(raw.shape),
                                   ALU.add).then_inc(hi_done, 1)
                pool.wait_ge(hi_done, n + 1)
                pool.tensor_tensor(parts[:, LO], raw[:, :, :], f32(parts[:, HI]), ALU.subtract).then_inc(ready, 1)

            split(wq_raw, wq_s, wq_in, wq_ready, 0, 0)
            split(wk_raw, wk_s, wk_in, wk_ready, 0, 1)
            split(wv_raw, wv_s, wv_in, wv_ready, 0, 2)

            def pair(it, last):
                jobs = before(it, jobs_in)
                if not is_first(it):
                    pool.wait_ge(job_done, jobs + job_at(it, 0, ("o", 3)))
                split(wo_raw, wo_s, wo_in, wo_ready, it, it * 4 + 3)
                if not last:
                    pool.wait_ge(job_done, jobs + job_at(it, 1, ("v", 1)))
                    split(wv_raw, wv_s, wv_in, wv_ready, it + 1, it * 4 + 4)
                    pool.wait_ge(job_done, jobs + job_at(it, 2, ("qk", 1)))
                    split(wq_raw, wq_s, wq_in, wq_ready, it + 1, it * 4 + 5)
                    pool.wait_ge(job_done, jobs + job_at(it, 2, ("qk", 3)))
                    split(wk_raw, wk_s, wk_in, wk_ready, it + 1, it * 4 + 6)

            pair(0, False)
            with pool.Fori(1, LAST) as it:
                pair(it, False)
            pair(LAST, True)
            pool.wait_ge(job_taken, before(LAST, jobs_in) + job_at(LAST, UNITS - 2, ("bw", 0)))
            for n in range(NT):
                pool.wait_ge(norm_ready, NT + n + 1)
                pool.tensor_tensor(acc[:, n, :], acc[:, n, :], bias_s[:, :], ALU.add).then_inc(resid_ready, 1)

        @block.tensor
        def _(pe):
            def turn_norm(first, n, kd, before, dst):
                pe.wait_ge(norm_ready, before + first + n)
                for j in range(n):
                    mm = pe.transpose(dst[:, j * P:(j + 1) * P], norm[:, (first + j) % 4, kd * P:(kd + 1) * P], ident[:, :])
                return mm

            def project_qk(part, k, dst):
                w_s = wq_s if part < 2 else wk_s
                b, hh, c = k // 2, k % 2, part % 2
                cols = slice(b * S + c * BANK, b * S + (c + 1) * BANK)
                for i, (kd, (a, m)) in enumerate([(kd, p) for kd in range(KD) for p in PASSES]):
                    mm = pe.matmul(dst, w_s[:, a, kd, hh * E:(hh + 1) * E], xT[:, m, kd, cols],
                                   start=(i == 0), stop=(i == 3 * KD - 1))
                return mm

            def project_v(c, b, dst):
                for j in range(2):
                    tok = b * S + (2 * c + j) * P
                    for i, (kd, (a, m)) in enumerate([(kd, p) for kd in range(KD) for p in PASSES]):
                        mm = pe.matmul(dst[:, j * 2 * E:(j + 1) * 2 * E], xT[:, a, kd, tok:tok + P], wv_s[:, m, kd, :],
                                       start=(j == 0 and i == 0), stop=(i == 3 * KD - 1), skip_group_check=True)
                return mm

            def weighted_v(half, k, dst, keys):
                b, hh = k // 2, k % 2
                pT = pT1 if half else pT0
                n_keys = HALF * (half + 1)
                for j in keys:
                    lo = min(max(0, j - half * HALF) * P, BANK - 2 * P)
                    for i, (a, m) in enumerate(PASSES):
                        mm = pe.matmul(dst[:, lo:BANK], v[:, b, a, j, hh * E:(hh + 1) * E], pT[:, m, j, lo:BANK],
                                       start=(j == 0 and i == 0), stop=(j == n_keys - 1 and i == 2))
                return mm

            def weighted_v_tiles(c, k, dst):
                q = (2 * c - HALF) * P
                n_keys = 2 * c + 2
                for j in range(n_keys):
                    for i, (a, m) in enumerate(PASSES):
                        mm = pe.matmul(dst[:, 0:2 * P], v[:, k // 2, a, j, (k % 2) * E:(k % 2 + 1) * E],
                                       pT1[:, m, j, q:q + 2 * P], start=(j == 0 and i == 0), stop=(j == n_keys - 1 and i == 2))
                return mm

            def project_o(c, hh, dst):
                for j in range(2):
                    tok = (2 * c + j) * P
                    for i, (a, m) in enumerate(PASSES):
                        mm = pe.matmul(dst[:, j * D:(j + 1) * D], zT[:, a, tok:tok + P], wo_s[:, m, hh, :],
                                       start=(j == 0 and i == 0), stop=(i == 2), skip_group_check=True)
                return mm

            def project_ffn(c, dst):
                for j in range(2):
                    tok = (2 * c + j) * P
                    for i, (kd, a) in enumerate([(kd, a) for kd in range(KD) for a in (LO, HI)]):
                        mm = pe.matmul(dst[:, j * D:(j + 1) * D], xT[:, a, kd, tok:tok + P], wf_s[:, kd, :],
                                       start=(j == 0 and i == 0), stop=(i == 3), skip_group_check=True)
                return mm

            def score_tile(k, t):
                par = k % 2
                first = first_column(t)
                width = max(2, t + 1) * P
                for c in sorted({0, BANK - first}):
                    n = min(BANK - first, width) if c == 0 else width - c
                    if n <= 0:
                        continue
                    diagonal = c <= t * P < c + n
                    for i, (a, m) in enumerate(PASSES):
                        mm = pe.matmul(scores[:, t % 2, first + c:first + c + n], qT[:, par, a, t * P:(t + 1) * P],
                                       kT[:, par, m, c:c + n], start=(i == 0), stop=(i == 2 and not diagonal))
                    if diagonal:
                        own = scores[:, t % 2, first + t * P:first + (t + 1) * P]
                        mm = pe.matmul(own, ident_b[:, :], mask[:, :], start=False, stop=True)
                mm.then_inc(scores_ready, 1)

            def turn_tile(t, g, g0):
                for n in range(banks(t)):
                    if not isinstance(g0, int) or g0 + g + n >= 2:
                        pe.wait_ge(plo_ready, g0 + (g + n - 1))
                    for j in range(4 * n, min(4 * n + 4, t + 1)):
                        mm = pe.transpose(turned[:, (g + n) % 2, (j % 4) * P:(j % 4 + 1) * P],
                                          probs[:, t % 2, j * P:(j + 1) * P], ident[:, :])
                    mm.then_inc(turned_ready, 1)

            def run(item, n, jobs, parity, it, k, groups):
                kind, arg = item
                if kind in NO_JOB and kind != "pv_part":
                    return n
                dst = ring[:, (parity + n) % 2, :]
                if (kind, arg) == ("pv", 1):
                    pass
                elif not isinstance(jobs, int) or jobs + n >= 2:
                    pe.wait_ge(job_taken, jobs + (n - 1))
                if kind == "x":
                    mm = turn_norm(*arg, 0, dst)
                elif kind == "xf":
                    mm = turn_norm(*arg, NT, dst)
                elif kind == "qk0":
                    pe.wait_ge(job_taken, first_job("x", (4 * (arg % 2), 4, KD - 1)))
                    pe.wait_ge(wk_ready if arg >= 2 else wq_ready, 1)
                    mm = project_qk(arg, 0, dst)
                elif kind == "qk":
                    if k == UNITS - 1 and arg in (0, 2):
                        pe.wait_ge(wk_ready if arg else wq_ready, it + 2)
                    mm = project_qk(arg, (k + 1) % UNITS, dst)
                elif kind == "v0":
                    pe.wait_ge(job_taken, first_job("x", (4 * (arg // 2), 4, KD - 1)))
                    pe.wait_ge(wv_ready, 1)
                    mm = project_v(arg, 0, dst)
                elif kind == "v":
                    if is_first(it) and k < 2 and arg == 0:
                        pe.wait_ge(job_taken, first_job("x", (8 + 4 * k, 4, KD - 1)))
                    if k == 2 and arg == 0:
                        pe.wait_ge(wv_ready, it + 2)
                    mm = project_v(arg + 2 * (k % 2), (k // 2 + 1) % 2, dst)
                elif kind == "pv" and arg == 0:
                    pe.wait_ge(plo_ready, groups + (k * GROUPS + HALF))
                    if is_first(it) and k == 0:
                        pe.wait_ge(job_taken, first_job("v0", 1))
                    mm = weighted_v(0, k, dst, range(HALF))
                elif kind == "pv_part":
                    pe.wait_ge(plo_ready, groups + (k * GROUPS - 1))
                    if is_first(it) and k == 1:
                        pe.wait_ge(job_taken, first_job("v0", 3))
                    weighted_v(1, (k - 1) % UNITS, dst, range(HALF))
                    return n
                elif kind == "pv":
                    pe.wait_ge(plo_ready, groups + k * GROUPS)
                    mm = weighted_v(1, (k - 1) % UNITS, dst, range(HALF, QT))
                elif kind == "pv_q":
                    pe.wait_ge(plo_ready, groups + (UNITS - 1) * GROUPS + sum(banks(t) for t in range(2 * arg + 2)))
                    mm = weighted_v_tiles(arg, UNITS - 1, dst)
                elif kind == "o":
                    if k == 1 and arg == 0:
                        pe.wait_ge(wo_ready, it + 1)
                    if arg == 0 and k > 0:
                        pe.wait_ge(job_taken, jobs + job_at(it, k - 1, ("pv", 0)))
                    elif arg == 0:
                        pe.wait_ge(job_taken, jobs - (jobs_in(flat(UNIT)) - job_at(1, 0, ("pv", 0))))
                    elif arg == 2:
                        pe.wait_ge(job_taken, jobs + job_at(it, k, ("pv", 1)))
                    mm = project_o(arg, (k - 1) % 2, dst)
                elif kind == "o_own":
                    pe.wait_ge(job_taken, z_jobs[arg])
                    mm = project_o(arg, (UNITS - 1) % 2, dst)
                elif kind == "wsum":
                    pe.wait_ge(wabs_ready, 1)
                    mm = pe.matmul(dst[:, 0:1], one[:, :].broadcast_to([P, P]), wabs[:, :], start=True, stop=True)
                elif kind == "bw":
                    pe.wait_ge(wf_ready, 1)
                    pe.wait_ge(small_in, 48)
                    for kd in range(KD):
                        mm = pe.matmul(dst[:, 0:D], beta_s[:, kd:kd + 1].broadcast_to([P, P]), f32(wf_s[:, kd, :]),
                                       start=(kd == 0), stop=(kd == KD - 1))
                else:
                    pe.wait_ge(job_taken, xf_jobs[arg])
                    mm = project_ffn(arg, dst)
                mm.then_inc(job_done, 1)
                if kind == "xf":
                    for c in range(arg[0] // 2, (arg[0] + arg[1]) // 2):
                        xf_jobs[c] = jobs + n + 1
                elif kind == "pv" and arg == 0:
                    z_jobs[0] = z_jobs[1] = jobs + n + 1
                elif kind == "pv_q":
                    z_jobs[arg] = jobs + n + 1
                return n + 1

            z_jobs, xf_jobs = {}, {}

            pe.wait_ge(const_ready, 6)
            for _ in range(WARM_UP):
                pe.matmul(scores[:, 1, 0:P], ident_b[:, :], mask[:, :], start=True, stop=True)

            n = 0
            for item in PROLOGUE:
                n = run(item, n, 0, 0, 0, None, 0)
            pe.wait_ge(job_taken, max(first_job("qk0", 0), first_job("qk0", 2)))
            score_tile(0, 0)

            def pair(it, last):
                jobs, groups, tiles = before(it, jobs_in), it * (UNITS * GROUPS), it * (UNITS * QT)
                n, g = 0, 0
                for k in range(UNITS):
                    for t, slot in enumerate(plan(it, k)):
                        for item in in_full(slot):
                            if item == TURN:
                                pe.wait_ge(probs_ready, tiles + (k * QT + t + 1))
                                turn_tile(t, g, groups)
                            elif item != NEXT:
                                n = run(item, n, jobs, odd(it), it, k, groups)
                            elif t < QT - 1:
                                if is_first(it) and k == 0 and t + 1 == HALF:
                                    pe.wait_ge(job_taken, max(first_job("qk0", 1), first_job("qk0", 3)))
                                score_tile(k, t + 1)
                            elif not last or k < UNITS - 1:
                                pe.wait_ge(job_taken, jobs + job_at(it, k, ("qk", 3)))
                                score_tile((k + 1) % UNITS, 0)
                        g += banks(t)
                return jobs, n

            pair(0, False)
            with pe.Fori(1, LAST) as it:
                pair(it, False)
            jobs, n = pair(LAST, True)
            for item in EPILOGUE:
                n = run(item, n, jobs, odd(LAST), LAST, UNITS, LAST * UNITS * GROUPS)

        @block.scalar
        def _(act):
            def exp_tile(k, t, tile):
                act.wait_ge(max_ready, tile + 1)
                act.activation(probs[:, t % 2, 0:(t + 1) * P], scores[:, t % 2, score_columns(t)], ACT.Exp,
                               bias=negmax[:, t % 2:t % 2 + 1],
                               accum_out=rowsum[:, k % 2, t:t + 1]).then_inc(probs_ready, 1)

            def turned_hi(t, g, g0):
                pT = pT1 if t >= HALF else pT0
                q = (t % HALF) * P
                for n in range(banks(t)):
                    act.wait_ge(turned_ready, g0 + (g + n + 1))
                    w = min(4, t + 1 - 4 * n)
                    act.activation(pT[:, HI, 4 * n:4 * n + w, q:q + P],
                                   turned[:, (g + n) % 2, 0:w * P].rearrange("p (j q) -> p j q", q=P),
                                   ACT.Copy).then_inc(phi_ready, 1)

            lns = [0]

            def run(item, n, jobs, parity, k):
                kind, arg = item
                if kind in NO_JOB:
                    if kind == "stats":
                        lns[0] += 2
                    elif kind == "rstd":
                        f, m = arg
                        act.wait_ge(ln_step, lns[0])
                        variance = mv[:, f:f + m, 1]
                        if k is None:
                            ins = act.activation(std[:, f:f + m], variance, ACT.Sqrt, bias=eps[:, 0:1])
                        else:
                            ins = act.activation(std[:, f:f + m], variance, ACT.Sqrt, bias=eps[:, 1:2],
                                                 scale=1.0 + LN_EPS)
                        ins.then_inc(std_ready, 1)
                        lns[0] += 1
                    return n
                if kind in NO_SPLIT:
                    return n + 1
                src, scale = ring[:, (parity + n) % 2, :], 1.0
                if kind in ("x", "xf"):
                    f, m, kd = arg
                    dst = xT[:, HI, kd, f * P:(f + m) * P]
                    src = src[:, 0:m * P]
                    if kind == "xf":
                        scale = gamma_s[:, kd:kd + 1]
                elif kind in ("qk0", "qk"):
                    k_next = 0 if kind == "qk0" else (k + 1) % 2
                    dst = (qT if arg < 2 else kT)[:, k_next, HI, (arg % 2) * BANK:(arg % 2 + 1) * BANK]
                    scale = SCALE if arg < 2 else 1.0
                elif kind in ("v0", "v"):
                    c, b = (arg, 0) if kind == "v0" else (arg + 2 * (k % 2), (k // 2 + 1) % 2)
                    dst = v[:, b, HI, 2 * c:2 * c + 2, :].rearrange("p a n -> p (a n)")
                elif kind == "pv_q":
                    dst, src = zT[:, HI, arg * 2 * P:(arg + 1) * 2 * P], src[:, 0:2 * P]
                else:
                    dst = zT[:, HI, arg * BANK:(arg + 1) * BANK]
                act.wait_ge(job_done, jobs + (n + 1))
                act.activation(dst, src, ACT.Copy, scale=scale).then_inc(jhi_ready, 1)
                return n + 1

            act.wait_ge(dve_const, 1)
            act.activation(unused[:, :], eps[:, 0:1], ACT.Sqrt, bias=eps[:, 0:1])
            pro = 0
            for item in PROLOGUE:
                pro = run(item, pro, 0, 0, None)
            exp_tile(0, 0, 0)

            def pair(it, last):
                jobs, groups, tiles = before(it, jobs_in), it * (UNITS * GROUPS), it * (UNITS * QT)
                n, g = 0, 0
                for k in range(UNITS):
                    for t, slot in enumerate(plan(it, k, UNIT_SCALAR)):
                        for item in in_full(slot):
                            if item == TURN:
                                turned_hi(t, g, groups)
                            elif item != NEXT:
                                n = run(item, n, jobs, odd(it), k)
                            elif t < QT - 1:
                                exp_tile(k, t + 1, tiles + (k * QT + t + 1))
                            elif not last or k < UNITS - 1:
                                exp_tile((k + 1) % UNITS, 0, tiles + (k + 1) * QT)
                        g += banks(t)
                return jobs, n

            pair(0, False)
            with act.Fori(1, LAST) as it:
                pair(it, False)
            jobs, n = pair(LAST, True)
            for item in EPILOGUE:
                n = run(item, n, jobs, odd(LAST), UNITS)

        @block.vector
        def _(dve):
            dve.memset(eps[:, 0:1], LN_EPS)
            dve.memset(eps[:, 1:2], LN_EPS * LN_EPS).then_inc(dve_const, 1)
            for a in (HI, LO):
                dve.memset(f32(pT1[:, a, HALF + 1, 0:P]), 0.0)
                dve.memset(f32(pT0[:, a, HALF - 1, BANK - 2 * P:BANK - P]), 0.0)
                dve.memset(f32(pT1[:, a, QT - 1, BANK - 2 * P:BANK - P]), 0.0)
            dve.memset(one[:, :], 1.0)

            def max_tile(t, tile):
                dve.wait_ge(scores_ready, tile + 1)
                dve.tensor_reduce(negmax[:, t % 2:t % 2 + 1], scores[:, t % 2, score_columns(t)], AX_X, ALU.max,
                                  negate=True).then_inc(max_ready, 1)

            def invert_sums(k, units):
                dve.wait_ge(probs_ready, units * QT)
                dve.reciprocal(inv[:, k % 2, :], rowsum[:, k % 2, :]).then_inc(inv_ready, 1)

            def turned_lo(t, g, g0):
                pT = pT1 if t >= HALF else pT0
                q = (t % HALF) * P
                for n in range(banks(t)):
                    dve.wait_ge(phi_ready, g0 + (g + n + 1))
                    w = min(4, t + 1 - 4 * n)
                    dve.tensor_tensor(pT[:, LO, 4 * n:4 * n + w, q:q + P],
                                      turned[:, (g + n) % 2, 0:w * P].rearrange("p (j q) -> p j q", q=P),
                                      f32(pT[:, HI, 4 * n:4 * n + w, q:q + P]), ALU.subtract).then_inc(plo_ready, 1)

            def add_o(c, k, src):
                for j in range(2):
                    t = 2 * c + j
                    tile = acc[:, (k // 2) * QT + t, :]
                    last = dve.scalar_tensor_tensor(out=tile, in0=src[:, j * D:(j + 1) * D],
                                                    scalar=inv[:, k % 2, t:t + 1], in1=tile,
                                                    op0=ALU.mult, op1=ALU.add)
                return last

            def ternary_threshold(src):
                return dve.tensor_scalar(thr[:, 0:1], src[:, 0:1], 0.5 / (D * D), 0.5 * Q_EPS, ALU.mult, ALU.add)

            def ternary_weight():
                dve.tensor_scalar(thr[:, 1:2], thr[:, 0:1], -1.0, None, ALU.mult).then_inc(tern_step, 1)
                dve.wait_ge(tern_step, 1)
                dve.tensor_scalar(wf_neg, wf_raw, thr[:, 1:2], None, ALU.is_lt).then_inc(tern_step, 1)
                dve.wait_ge(tern_step, 2)
                dve.scalar_tensor_tensor(out=wf_s[:, :, :], in0=wf_raw, scalar=thr[:, 0:1], in1=wf_neg,
                                         op0=ALU.is_gt, op1=ALU.subtract).then_inc(wf_ready, 1)

            lns = [0]
            stds = [0]

            def layernorm_item(kind, arg):
                f, m = arg
                if kind == "stats":
                    for t in range(f, f + m):
                        last = dve.bn_stats(stats[:, t, :], acc[:, t, :])
                    last.then_inc(ln_step, 1)
                    dve.wait_ge(ln_step, lns[0] + 1)
                    for t in range(f, f + m):
                        last = dve.bn_aggr(mv[:, t, :], stats[:, t, :])
                    last.then_inc(ln_step, 1)
                    lns[0] += 2
                elif kind == "rstd":
                    stds[0] += 1
                    dve.wait_ge(std_ready, stds[0])
                    dve.reciprocal(rstd[:, f:f + m], std[:, f:f + m]).then_inc(ln_step, 1)
                    lns[0] += 1
                    dve.wait_ge(ln_step, lns[0])
                else:
                    for t in range(f, f + m):
                        dve.tensor_scalar(norm[:, t % 4, :], acc[:, t, :], mv[:, t, 0:1], rstd[:, t:t + 1],
                                          ALU.subtract, ALU.mult).then_inc(norm_ready, 1)

            def run(item, n, s, jobs, splits, parity, it, k):
                kind, arg = item
                if kind == "wabs":
                    dve.wait_ge(wf_in, 16)
                    dve.tensor_reduce(wabs[:, :], wf_raw, AX_XY, ALU.add, apply_absolute_value=True).then_inc(wabs_ready, 1)
                    return n, s
                if kind == "pv_part":
                    return n, s
                if kind == "inv":
                    f, m = arg
                    dve.wait_ge(probs_ready, (PAIRS * UNITS - 1) * QT + f + m)
                    dve.reciprocal(inv[:, (UNITS - 1) % 2, f:f + m], rowsum[:, (UNITS - 1) % 2, f:f + m]).then_inc(inv_ready, 1)
                    invs[0] += 1
                    dve.wait_ge(inv_ready, invs[0])
                    return n, s
                if kind in NO_JOB:
                    if kind == "stats" and k is not None:
                        dve.wait_ge(job_taken, jobs + n)
                    layernorm_item(kind, arg)
                    return n, s
                src = ring[:, (parity + n) % 2, :]
                if kind in NO_SPLIT:
                    if kind == "o" and arg == 0:
                        dve.wait_ge(inv_ready, it * UNITS + k)
                    dve.wait_ge(job_done, jobs + (n + 1))
                    if kind == "o":
                        add_o(arg, (k - 1) % UNITS, src).then_inc(job_taken, 1)
                    elif kind == "o_own":
                        add_o(arg, UNITS - 1, src).then_inc(job_taken, 1)
                    elif kind == "wsum":
                        ternary_threshold(src).then_inc(job_taken, 1)
                        dve.wait_ge(job_taken, jobs + (n + 1))
                        ternary_weight()
                    elif kind == "bw":
                        dve.wait_ge(small_in, 48)
                        dve.tensor_tensor(bias_s[:, :], src[:, 0:D], bias_s[:, :], ALU.add).then_inc(job_taken, 1)
                    else:
                        tiles = acc[:, 2 * arg:2 * arg + 2, :].rearrange("p n d -> p (n d)")
                        dve.wait_ge(resid_ready, 2 * arg + 2)
                        dve.tensor_tensor(tiles, src, tiles, ALU.add).then_inc(job_taken, 1)
                    return n + 1, s
                scale = None
                if kind in ("x", "xf"):
                    f, m, kd = arg
                    hi, lo = (xT[:, a, kd, f * P:(f + m) * P] for a in (HI, LO))
                    src = src[:, 0:m * P]
                    if kind == "xf":
                        scale = gamma_s[:, kd:kd + 1]
                elif kind in ("qk0", "qk"):
                    k_next = 0 if kind == "qk0" else (k + 1) % 2
                    hi, lo = ((qT if arg < 2 else kT)[:, k_next, a, (arg % 2) * BANK:(arg % 2 + 1) * BANK] for a in (HI, LO))
                    scale = SCALE if arg < 2 else None
                elif kind in ("v0", "v"):
                    c, b = (arg, 0) if kind == "v0" else (arg + 2 * (k % 2), (k // 2 + 1) % 2)
                    hi, lo = (v[:, b, a, 2 * c:2 * c + 2, :].rearrange("p a n -> p (a n)") for a in (HI, LO))
                elif kind == "pv_q":
                    hi, lo = (zT[:, a, arg * 2 * P:(arg + 1) * 2 * P] for a in (HI, LO))
                    src = src[:, 0:2 * P]
                else:
                    hi, lo = (zT[:, a, arg * BANK:(arg + 1) * BANK] for a in (HI, LO))
                dve.wait_ge(jhi_ready, splits + (s + 1))
                if scale is None:
                    ins = dve.tensor_tensor(lo, src, f32(hi), ALU.subtract)
                else:
                    ins = dve.scalar_tensor_tensor(out=lo, in0=src, scalar=scale, in1=f32(hi),
                                                   op0=ALU.mult, op1=ALU.subtract)
                ins.then_inc(job_taken, 1)
                return n + 1, s + 1

            invs = [PAIRS * UNITS - 1]
            n, s = 0, 0
            for item in PROLOGUE:
                if item[0] == "stats":
                    f, m = item[1]
                    for g in range(f // 4, (f + m) // 4):
                        dve.wait_ge(x_in[g], 16)
                n, s = run(item, n, s, 0, 0, 0, 0, None)
            max_tile(0, 0)

            def pair(it, last):
                jobs, splits = before(it, jobs_in), before(it, splits_in)
                groups, tiles = it * (UNITS * GROUPS), it * (UNITS * QT)
                n, s, g = 0, 0, 0
                for k in range(UNITS):
                    for t, slot in enumerate(plan(it, k, UNIT_VECTOR)):
                        if t == 0 and (k > 0 or not is_first(it)):
                            invert_sums((k - 1) % UNITS, it * UNITS + k)
                        for item in in_full(slot):
                            if item == TURN:
                                turned_lo(t, g, groups)
                            elif item != NEXT:
                                n, s = run(item, n, s, jobs, splits, odd(it), it, k)
                            elif t < QT - 1:
                                max_tile(t + 1, tiles + (k * QT + t + 1))
                            elif not last or k < UNITS - 1:
                                max_tile(0, tiles + (k + 1) * QT)
                        g += banks(t)
                return jobs, splits, n, s

            pair(0, False)
            with dve.Fori(1, LAST) as it:
                pair(it, False)
            jobs, splits, n, s = pair(LAST, True)
            for item in EPILOGUE:
                n, s = run(item, n, s, jobs, splits, odd(LAST), LAST, UNITS)

_INS = ("x", "wq", "wk", "wv", "wo", "wf", "gamma", "beta", "bias")


def kernel(L0_attn_x, L0_attn_W_Q, L0_attn_W_K, L0_attn_W_V, L0_attn_W_O, L0_ffn_weight, L0_ffn_bias,
           L0_ffn_ln_gamma, L0_ffn_ln_beta):
    import numpy as np
    import concourse.bacc as bacc
    from concourse.bass_utils import run_bass_kernel_spmd as run

    B, S, D = L0_attn_x.shape
    H, E, _ = L0_attn_W_Q.shape

    def in_weight(w):
        return np.ascontiguousarray(np.asarray(w).reshape(H // 2, 2, E, D // P, P).transpose(0, 4, 3, 1, 2)
                                    .reshape(H // 2, P, D // P, 2 * E))

    host = {
        "x": np.asarray(L0_attn_x).reshape(B * S, D),
        "wq": in_weight(L0_attn_W_Q),
        "wk": in_weight(L0_attn_W_K),
        "wv": in_weight(L0_attn_W_V),
        "wo": np.ascontiguousarray(np.asarray(L0_attn_W_O).reshape(H // 2, 2, D, E).transpose(0, 3, 1, 2)),
        "wf": np.ascontiguousarray(np.asarray(L0_ffn_weight).reshape(D, D // P, P).transpose(2, 1, 0)),
        "gamma": np.ascontiguousarray(np.asarray(L0_ffn_ln_gamma).reshape(D // P, P).T),
        "beta": np.ascontiguousarray(np.asarray(L0_ffn_ln_beta).reshape(D // P, P).T),
        "bias": np.asarray(L0_ffn_bias),
    }
    nc = bacc.Bacc("TRN2", target_bir_lowering=False, num_devices=1)
    args = [nc.dram_tensor(f"in_{n}", host[n].shape, mybir.dt.from_np(host[n].dtype), kind="ExternalInput").ap()
            for n in _INS]
    out = nc.dram_tensor("out", (B * S, D), F32, kind="ExternalOutput").ap()
    attention_ffn(nc, *args, out)
    r = run(nc, [{f"in_{n}": host[n] for n in _INS}], core_ids=[0])
    return r.results[0]["out"].reshape(B, S, D)
```
